# Optimizing a Trainium2 kernel written in Bass

```python
import numpy as np
import jax
import jax.numpy as jnp

def _softmax(x, axis=-1):
    return jax.nn.softmax(x, axis=axis)

def _gelu(x):
    return jax.nn.gelu(x, approximate=True)

def _silu(x):
    return jax.nn.silu(x)

def _sigmoid(x):
    return jax.nn.sigmoid(x)

def _layernorm(x, axis=-1, eps=1e-05):
    m = jnp.mean(x, axis=axis, keepdims=True)
    v = jnp.var(x, axis=axis, keepdims=True)
    return (x - m) / jnp.sqrt(v + eps)

def _scatter_add(tgt, idx, src, axis=0):
    return tgt.at[idx].add(src)

def _segment_sum(src, seg, n):
    return jax.ops.segment_sum(src, seg, n)
kernel_name = 'mk_pixart_resid_d1_seqx_r2_48d257'

def setup_inputs(seed: int=0):
    np.random.seed(seed)
    _w = jnp.asarray

    def _rec_inputs():
        import jax
        import jax.numpy as jnp
        _rk = jax.random.key(seed)
        x = 7.22e-05 + 1 * jax.random.normal(jax.random.fold_in(_rk, 1), (8, 512, 512), jnp.float32)
        _lenS = 512 - jax.random.randint(jax.random.fold_in(_rk, 7), (8,), 0, max(1, 512 // 4) + 1, jnp.int32)
        _lenS2 = 512 - jax.random.randint(jax.random.fold_in(_rk, 8), (8,), 0, max(1, 512 // 4) + 1, jnp.int32)
        _ctx_1024P = jax.random.normal(jax.random.fold_in(_rk, 11), (8, 16, 512), jnp.float32)
        _ctx_1024c = jax.random.dirichlet(jax.random.fold_in(_rk, 511), 0.3 * jnp.ones((16,), jnp.float32), (8, 512))
        _ctx_1024t = jnp.einsum('bsk,bkd->bsd', _ctx_1024c, _ctx_1024P)
        _ctx_1024t = _ctx_1024t * jax.lax.rsqrt(jnp.mean(jnp.square(_ctx_1024t)) + 1e-12) * 0.953939
        ctx_1024 = 5.54337e-07 + 0.0180436 * (_ctx_1024t + 0.3 * jax.random.normal(jax.random.fold_in(_rk, 611), (8, 512, 512), jnp.float32))
        cond_1024 = 0.000192168 + 0.0182672 * jax.random.normal(jax.random.fold_in(_rk, 12), (8, 512), jnp.float32)
        return (x, ctx_1024, cond_1024)
    x, ctx_1024, cond_1024 = _rec_inputs()

    def _L0_xcond_setup():
        import jax, jax.numpy as jnp
        import numpy as np
        B, S, H, L = (4, 1024, 512, 4)
        CLAMP_LO, CLAMP_HI = (1e-08, 1.0 - 1e-08)
        LN_EPS = 1e-05

        def _linear_scan(a, b):

            def combine(left, right):
                al, bl = left
                ar, br = right
                return (ar * al, ar * bl + br)
            _, h = jax.lax.associative_scan(combine, (a, b), axis=1)
            return h

        def _mingru(x, Wz, bz, Wh, bh):
            z = jax.nn.sigmoid(jnp.einsum('bsi,hi->bsh', x, Wz) + bz)
            h_tilde = jnp.tanh(jnp.einsum('bsi,hi->bsh', x, Wh) + bh)
            a = jnp.clip(1.0 - z, CLAMP_LO, CLAMP_HI)
            return _linear_scan(a, z * h_tilde)

        def _layernorm(x, gamma, beta):
            mu = jnp.mean(x, axis=-1, keepdims=True)
            var = jnp.mean(jnp.square(x - mu), axis=-1, keepdims=True)
            return (x - mu) * jax.lax.rsqrt(var + LN_EPS) * gamma + beta

        def _stack(x, Wz, bz, Wh, bh, gamma, beta):
            h = x
            for i in range(L):
                h_new = _mingru(h, Wz[i], bz[i], Wh[i], bh[i])
                if i > 0:
                    h_new = h_new + h
                h = _layernorm(h_new, gamma, beta)
            return h
        key = jax.random.key(seed)
        ks = jax.random.split(key, 13)
        s = 1.0 / np.sqrt(H)
        u = lambda k, shape: jax.random.uniform(k, shape, jnp.float32, -s, s)
        return {'x': jax.random.normal(ks[0], (B, S, H), jnp.float32), 'fwd_Wz': u(ks[1], (L, H, H)), 'fwd_bz': u(ks[2], (L, H)), 'fwd_Wh': u(ks[3], (L, H, H)), 'fwd_bh': u(ks[4], (L, H)), 'bwd_Wz': u(ks[5], (L, H, H)), 'bwd_bz': u(ks[6], (L, H)), 'bwd_Wh': u(ks[7], (L, H, H)), 'bwd_bh': u(ks[8], (L, H)), 'fusion_W': u(ks[9], (H, 2 * H)), 'fusion_b': u(ks[10], (H,)), 'ln_gamma': jnp.ones((H,), jnp.float32), 'ln_beta': jnp.zeros((H,), jnp.float32)}
    _L0_xcond_all = _L0_xcond_setup()
    _L0_xcond_in = {k: v for k, v in _L0_xcond_all.items() if k in ('fusion_W', 'fusion_b', 'ln_gamma', 'ln_beta')}
    del _L0_xcond_all

    def _L0_ffn_setup():
        import jax, jax.numpy as jnp
        import numpy as np
        EPS = 1e-06
        LN_EPS = 1e-05

        def _absmean_core(W):
            gamma = jnp.mean(jnp.abs(W)) + EPS
            Ws = W / gamma
            Wq = jnp.sign(Ws) * jnp.minimum(jnp.round(jnp.abs(Ws)), 1.0)
            return (Wq, gamma)

        @jax.custom_vjp
        def absmean(W):
            return _absmean_core(W)[0]

        def _absmean_fwd(W):
            Wq, gamma = _absmean_core(W)
            return (Wq, gamma)

        def _absmean_bwd(gamma, g):
            return (g / gamma,)
        absmean.defvjp(_absmean_fwd, _absmean_bwd)

        def layernorm(x, w, b, eps=LN_EPS):
            mu = jnp.mean(x, axis=-1, keepdims=True)
            var = jnp.mean((x - mu) ** 2, axis=-1, keepdims=True)
            return (x - mu) * jax.lax.rsqrt(var + eps) * w + b
        key = jax.random.key(seed)
        k1, k2, k3 = jax.random.split(key, 3)
        d, h = (512, 2048)
        B, T = (8, 1024)
        return {'x': jax.random.normal(k1, (B, T, d), jnp.float32), 'W_fc': jax.random.normal(k2, (h, d), jnp.float32), 'ln_w': jnp.ones((h,), jnp.float32), 'ln_b': jnp.zeros((h,), jnp.float32), 'W_proj': jax.random.normal(k3, (d, h), jnp.float32)}
    _L0_ffn_all = _L0_ffn_setup()
    _L0_ffn_in = {k: v for k, v in _L0_ffn_all.items() if k in ('W_fc', 'ln_w', 'ln_b', 'W_proj')}
    del _L0_ffn_all
    return {'x': x, 'ctx_1024': ctx_1024, 'cond_1024': cond_1024, 'L0_xcond_fusion_W': _L0_xcond_in['fusion_W'], 'L0_xcond_fusion_b': _L0_xcond_in['fusion_b'], 'L0_xcond_ln_gamma': _L0_xcond_in['ln_gamma'], 'L0_xcond_ln_beta': _L0_xcond_in['ln_beta'], 'L0_ffn_W_fc': _L0_ffn_in['W_fc'], 'L0_ffn_ln_w': _L0_ffn_in['ln_w'], 'L0_ffn_ln_b': _L0_ffn_in['ln_b'], 'L0_ffn_W_proj': _L0_ffn_in['W_proj']}

def reference(x, ctx_1024, cond_1024, L0_xcond_fusion_W, L0_xcond_fusion_b, L0_xcond_ln_gamma, L0_xcond_ln_beta, L0_ffn_W_fc, L0_ffn_ln_w, L0_ffn_ln_b, L0_ffn_W_proj):
    import jax
    import jax.numpy as jnp

    def _L0_xcond_ref(x, fwd_Wz, fwd_bz, fwd_Wh, fwd_bh, bwd_Wz, bwd_bz, bwd_Wh, bwd_bh, fusion_W, fusion_b, ln_gamma, ln_beta):
        import jax, jax.numpy as jnp
        import numpy as np
        B, S, H, L = (4, 1024, 512, 4)
        CLAMP_LO, CLAMP_HI = (1e-08, 1.0 - 1e-08)
        LN_EPS = 1e-05

        def _linear_scan(a, b):

            def combine(left, right):
                al, bl = left
                ar, br = right
                return (ar * al, ar * bl + br)
            _, h = jax.lax.associative_scan(combine, (a, b), axis=1)
            return h

        def _mingru(x, Wz, bz, Wh, bh):
            z = jax.nn.sigmoid(jnp.einsum('bsi,hi->bsh', x, Wz) + bz)
            h_tilde = jnp.tanh(jnp.einsum('bsi,hi->bsh', x, Wh) + bh)
            a = jnp.clip(1.0 - z, CLAMP_LO, CLAMP_HI)
            return _linear_scan(a, z * h_tilde)

        def _layernorm(x, gamma, beta):
            mu = jnp.mean(x, axis=-1, keepdims=True)
            var = jnp.mean(jnp.square(x - mu), axis=-1, keepdims=True)
            return (x - mu) * jax.lax.rsqrt(var + LN_EPS) * gamma + beta

        def _stack(x, Wz, bz, Wh, bh, gamma, beta):
            h = x
            for i in range(L):
                h_new = _mingru(h, Wz[i], bz[i], Wh[i], bh[i])
                if i > 0:
                    h_new = h_new + h
                h = _layernorm(h_new, gamma, beta)
            return h
        h_fwd = _stack(x, fwd_Wz, fwd_bz, fwd_Wh, fwd_bh, ln_gamma, ln_beta)
        h_bwd = _stack(jnp.flip(x, axis=1), bwd_Wz, bwd_bz, bwd_Wh, bwd_bh, ln_gamma, ln_beta)
        h_bwd = jnp.flip(h_bwd, axis=1)
        h_comb = jnp.concatenate([h_fwd, h_bwd], axis=-1)
        return jnp.einsum('bsi,hi->bsh', h_comb, fusion_W) + fusion_b

    def _L0_ffn_ref(x, W_fc, ln_w, ln_b, W_proj):
        import jax, jax.numpy as jnp
        import numpy as np
        EPS = 1e-06
        LN_EPS = 1e-05

        def _absmean_core(W):
            gamma = jnp.mean(jnp.abs(W)) + EPS
            Ws = W / gamma
            Wq = jnp.sign(Ws) * jnp.minimum(jnp.round(jnp.abs(Ws)), 1.0)
            return (Wq, gamma)

        @jax.custom_vjp
        def absmean(W):
            return _absmean_core(W)[0]

        def _absmean_fwd(W):
            Wq, gamma = _absmean_core(W)
            return (Wq, gamma)

        def _absmean_bwd(gamma, g):
            return (g / gamma,)
        absmean.defvjp(_absmean_fwd, _absmean_bwd)

        def layernorm(x, w, b, eps=LN_EPS):
            mu = jnp.mean(x, axis=-1, keepdims=True)
            var = jnp.mean((x - mu) ** 2, axis=-1, keepdims=True)
            return (x - mu) * jax.lax.rsqrt(var + eps) * w + b
        h = jnp.einsum('btd,hd->bth', x, absmean(W_fc))
        h = jax.nn.gelu(h, approximate=False)
        h = layernorm(h, ln_w, ln_b)
        return jnp.einsum('bth,dh->btd', h, absmean(W_proj))
    x = x + _L0_xcond_ref(_layernorm(x, axis=-1), ctx_1024, cond_1024, ctx_1024, cond_1024, ctx_1024, cond_1024, ctx_1024, cond_1024, L0_xcond_fusion_W, L0_xcond_fusion_b, L0_xcond_ln_gamma, L0_xcond_ln_beta)
    x = x + _L0_ffn_ref(_layernorm(x, axis=-1), L0_ffn_W_fc, L0_ffn_ln_w, L0_ffn_ln_b, L0_ffn_W_proj)
    return x

_drawn_inputs = setup_inputs


def setup_inputs(seed=0):
    import zlib

    import numpy as np

    out = dict(_drawn_inputs(seed))
    spreads = {'L0_xcond_ln_gamma': (1.0, 0.2),
     'L0_xcond_ln_beta': (0.0, 0.1),
     'L0_ffn_ln_w': (1.0, 0.2),
     'L0_ffn_ln_b': (0.0, 0.1)}
    factors = {}
    for name, (base, spread) in spreads.items():
        noise = np.random.default_rng([zlib.crc32(name.encode()), seed]).standard_normal(out[name].shape)
        drawn = base * np.exp(spread * noise) if base else spread * noise
        out[name] = jnp.asarray(drawn.astype(out[name].dtype))
    for name, factor in factors.items():
        out[name] = (out[name] * factor).astype(out[name].dtype)
    return out
```

```python
from contextlib import ExitStack

import concourse.bass as bass
from concourse import mybir

F32 = mybir.dt.float32
F32R = mybir.dt.float32r
ALU = mybir.AluOpType
ACT = mybir.ActivationFunctionType
AX_X = mybir.AxisListType.X
RADD = bass.bass_isa.ReduceOp.add

NB = 8
S = 512
HID = 2048
L = 4
KC = 4
EPS = 1e-5
T = 14.0
U = 21.0


class Op:

    def __init__(self, eng, fn, waits, after, sem, key, cost):
        self.eng, self.fn, self.waits, self.after, self.sem = eng, fn, waits, after, sem
        self.key, self.cost = key, cost
        self.at = None
        self.used = False


def flatten(w):
    if w is None:
        return []
    if isinstance(w, (list, tuple)):
        return [o for x in w for o in flatten(x)]
    return [w]


class Queues:

    SLACK = {"pe": .3, "act": .1, "dve": .1, "pool": .1, "sp": 0.}
    REACH = {"pe": .2, "act": .15, "dve": .13, "pool": .13, "sp": 2.}

    def __init__(self, engines):
        self.ops = []
        self.order = {e: [] for e in engines}

    def add(self, eng, fn, waits, key, cost, sem=None, after=None):
        waits, after = flatten(waits), flatten(after)
        for o in waits:
            o.used = True
        op = Op(eng, fn, waits, after, sem, key, cost)
        self.ops.append(op)
        return op

    def arrange(self):
        left, users, ready = {}, {}, {e: [] for e in self.order}
        done = {}
        for n, o in enumerate(self.ops):
            o.n = n
            deps = {id(w): w for w in o.waits + o.after}
            left[o] = len(deps)
            for w in deps.values():
                users.setdefault(w, []).append(o)
            if not deps:
                ready[o.eng].append((0., o))
        free = {e: 0. for e in self.order}
        for _ in range(len(self.ops)):
            best = None
            for e, c in ready.items():
                if c:
                    start = min(max(free[e], t) for t, _ in c)
                    if best is None or start < best[0]:
                        best = (start, e)
            start, e = best
            limit = start + self.SLACK[e]
            t, o = min((x for x in ready[e] if max(free[e], x[0]) <= limit), key=lambda x: (x[1].key, x[1].n))
            ready[e].remove((t, o))
            begin = max(free[e], t)
            hold = .08 if e == "sp" else o.cost
            free[e] = begin + hold
            done[o] = begin + o.cost + self.REACH[e]
            self.order[e].append(o)
            for u in users.get(o, []):
                left[u] -= 1
                if not left[u]:
                    same = [begin + o.cost if w.eng == u.eng == "pe" else done[w] for w in u.waits]
                    ready[u.eng].append((max([0.] + same), u))

    def count(self):
        total = {}
        for eng, ops in self.order.items():
            for o in ops:
                if o.used or o.sem:
                    name = o.sem or eng
                    total[name] = total.get(name, 0) + (16 if o.sem else 1)
                    o.at = (name, total[name])
        return total

    def emit(self, eng, e, sems):
        seen = {}
        for o in self.order[eng]:
            need = {}
            for w in o.waits:
                name, value = w.at
                need[name] = max(need.get(name, 0), value)
            for name, value in need.items():
                if seen.get(name, 0) < value:
                    e.wait_ge(sems[name], value)
                    seen[name] = value
            last = o.fn(e)
            if o.at:
                last.then_inc(sems[o.at[0]], 16 if o.sem else 1)


class Ring:

    def __init__(self, n, first=None):
        self.n, self.i = n, 0
        self.free = list(first) if first else [None] * n

    def take(self):
        i = self.i % self.n
        self.i += 1
        w = self.free[i]() if callable(self.free[i]) else self.free[i]
        assert w != "held", "a buffer is taken before its release is planned"
        self.free[i] = "held"
        return i, w

    def give(self, i, *ops):
        self.free[i] = list(ops)


def pixart_block(nc, x, wt, cond, fwt, fb, gamma, beta, fct, lnw, lnb, pjt, out):
    hs = nc.dram_tensor("hs_scratch", [NB * 4, 128, 2, KC, 128], F32, kind="Internal").ap()
    q = Queues(["pe", "act", "dve", "pool", "sp"])
    ctx, p1, p2 = ExitStack(), ExitStack(), ExitStack()

    def sb(stack, name, shape, dt=F32):
        return stack.enter_context(nc.sbuf_tensor(name, shape, dt))

    now = [-30.]

    def pe(fn, *w, c=2.6, after=None):
        return q.add("pe", fn, w, now[0], c, after=after)

    def act(fn, *w, c=.57):
        return q.add("act", fn, w, now[0], c)

    def dve(fn, *w, c=.6):
        return q.add("dve", fn, w, now[0], c)

    def pool(fn, *w, c=1.23):
        return q.add("pool", fn, w, now[0], c)

    def dma(sem, fn, *w, c=3.):
        return q.add("sp", fn, w, now[0], c, sem=sem)

    plan = []
    made = [0]

    def at(t, fn):
        made[0] += 1
        plan.append((-t, -made[0], fn))

    ident = sb(ctx, "ident", [128, 128])
    nhalf = sb(ctx, "nhalf", [128, 4])
    tiny = sb(ctx, "tiny", [128, 1])
    condt = sb(ctx, "condt", [128, L, KC])
    gam = sb(ctx, "gam", [128, KC])
    bet = sb(ctx, "bet", [128, KC])
    asum = sb(ctx, "asum", [128, 32])
    ssum = sb(ctx, "ssum", [128, 2])
    tot = sb(ctx, "tot", [128, 2])
    th = sb(ctx, "th", [128, 2])
    nth = sb(ctx, "nth", [128, 2])
    NST = 4
    bn = sb(ctx, "bn", [128, NST, 4, 6])
    mv = sb(ctx, "mv", [128, NST, 4, 2])
    ve = sb(ctx, "ve", [128, NST, 4])
    rs = sb(ctx, "rs", [128, NST, 4])
    nb = sb(ctx, "nb", [128, NST, 4])
    stg = sb(ctx, "stg", [128, 512])
    xbuf = sb(ctx, "xbuf", [128, 4, 512])

    WH, WL, AH, AL = [], [], [], []
    for l in range(L):
        WH.append(sb(p1, f"WH{l}", [128, KC, 512], F32R))
        WL.append(sb(p1, f"WL{l}", [128, KC, 512], F32R))
    for s in range(4):
        AH.append(sb(p1, f"AH{s}", [128, KC, S], F32R))
        AL.append(sb(p1, f"AL{s}", [128, KC, S], F32R))
    H = [sb(p1, f"H{s}", [128, KC, S]) for s in range(4)]
    ntok = [sb(p1, f"ntok{i}", [128, 4, 512]) for i in range(2)]
    zb = [sb(p1, f"zb{i}", [128, S]) for i in range(2)]
    hb = [sb(p1, f"hb{i}", [128, S]) for i in range(2)]
    ab = [sb(p1, f"ab{i}", [128, S]) for i in range(2)]
    fin = sb(p1, "fin", [128, KC, S])
    p1.close()

    FUH = sb(p2, "FUH", [128, 8, 512], F32R)
    FUL = sb(p2, "FUL", [128, 8, 512], F32R)
    FCA = sb(p2, "FCA", [128, 2, HID], F32R)
    hch = [sb(p2, f"hch{i}", [128, 8, 128], F32R) for i in range(2)]
    hcl = [sb(p2, f"hcl{i}", [128, 8, 128], F32R) for i in range(2)]
    PJ = sb(p2, "PJ", [128, 16, 512], F32R)
    FCB = sb(p2, "FCB", [128, 2, HID], F32R)
    hc = [sb(p2, f"hc{i}", [128, 8, 128]) for i in range(2)]
    xr = [sb(p2, f"xr{i}", [128, 512]) for i in range(2)]
    xf = [sb(p2, f"xf{i}", [128, 512]) for i in range(2)]
    xh = [sb(p2, f"xh{i}", [128, 4, 128], F32R) for i in range(2)]
    xl = [sb(p2, f"xl{i}", [128, 4, 128], F32R) for i in range(2)]
    wrow = sb(p2, "wrow", [128, HID])
    uth = [sb(p2, f"uth{i}", [128, 4, 128], F32R) for i in range(4)]
    utl = [sb(p2, f"utl{i}", [128, 4, 128], F32R) for i in range(4)]
    g = [sb(p2, f"g{i}", [128, HID]) for i in range(2)]
    x1 = [sb(p2, f"x1{i}", [128, 512]) for i in range(3)]
    n1 = [sb(p2, f"n1{i}", [128, 512]) for i in range(2)]
    fbb = sb(p2, "fbb", [128, 512])
    ob = [sb(p2, f"ob{i}", [128, 512]) for i in range(2)]
    cB = sb(p2, "cB", [128, 512])
    lnbt = sb(p2, "lnbt", [128, 16])
    bh = [sb(p2, f"bh{i}", [128, 2, 128], F32R) for i in range(2)]
    p2.close()

    PS = [ctx.enter_context(nc.psum_tensor(f"ps{i}", [128, 512], F32)) for i in range(8)]

    c_id0 = pool(lambda e: e.memset(ident[:], 0.0))
    c_id = pool(lambda e: e.affine_select(out=ident[:], in_=ident[:], compare_op=ALU.not_equal, fill=1.0,
                                          base=0, pattern=[[-1, 128]], channel_multiplier=1), c_id0)
    c_nh = pool(lambda e: e.memset(nhalf[:], -0.5))
    c_tiny = pool(lambda e: e.memset(tiny[:], 1e-8))

    x_v = x.rearrange("b (i p) d -> b p i d", p=128)
    fct_v = fct.rearrange("(k p) (c n) -> p k c n", p=128, n=512)
    pjt_v = pjt.rearrange("(k p) n -> p k n", p=128)
    fwt_v = fwt.rearrange("(k p) n -> p k n", p=128)

    jobs = [(0, 0, 0), (1, 0, 0), (0, 0, 1), (0, 1, 1), (1, 0, 1), (1, 1, 1)]
    for b in range(0, NB, 2):
        jobs += [(b, 0, 2), (b, 1, 2), (b + 1, 0, 2), (b + 1, 1, 2), (b, 0, 3), (b, 1, 3), (b + 1, 0, 3)]
        if b + 2 < NB:
            jobs += [(b + 2, 0, 0), (b + 1, 1, 3), (b + 2, 0, 1), (b + 3, 0, 0), (b + 2, 1, 1),
                     (b + 3, 0, 1), (b + 3, 1, 1)]
        else:
            jobs += [(b + 1, 1, 3)]
    base = {j: T * k for k, j in enumerate(jobs)}
    END = T * len(jobs)

    gate = Ring(2)
    t1r = Ring(4)
    t2r = Ring(2)
    stat = Ring(NST)
    ntr = Ring(2)
    chr_ = Ring(2)
    a_rdy, h_rdy = [None] * 4, [None] * 4
    a_used, h_used = [None] * 4, [None] * 4
    mm_done = {}
    hs_done = {}
    fin_free = [None]

    ld_x = {0: dma("d_xb", lambda e: e.dma_start(xbuf[:], x_v[0]))}
    raw = [H[1], H[2], H[3], fin]
    w_ld = []
    for l in range(L):
        w_ld.append(dma(f"d_w{l}", lambda e, l=l: e.dma_start(raw[l][:], wt[l].rearrange("(k p) n -> p k n", p=128))))
        if l == 0:
            ld_c = dma("d_c0", lambda e: e.dma_start(condt[:], cond))
            ld_g = dma("d_c1", lambda e: e.dma_start(gam[:], gamma))
            ld_b = dma("d_c2", lambda e: e.dma_start(bet[:], beta))
    w_rdy = [None] * L

    def split_w(l):
        hi = dve(lambda e: e.tensor_copy(WH[l][:], raw[l][:]), w_ld[l], c=1.14)
        lo = dve(lambda e: e.tensor_tensor(WL[l][:], raw[l][:], WH[l][:].bitcast(F32), ALU.subtract), hi, c=2.2)
        w_rdy[l] = [hi, lo]
        if l < 3:
            h_used[l + 1] = [lo]
        else:
            fin_free[0] = [lo]

    for l in range(L):
        at(-10.5 if l == 0 else 1 + 3.5 * (l - 1), lambda l=l: split_w(l))

    def inv_std(r, lo, hi, aggr, want_nb):
        o = dve(lambda e: e.tensor_scalar(ve[:, r, lo:hi], mv[:, r, lo:hi, 1], EPS, None, ALU.add), aggr, c=.07)
        inv = pool(lambda e: e.tensor_tensor(rs[:, r, lo:hi], ve[:, r, lo:hi], nhalf[:, lo:hi], ALU.pow), o, c_nh,
                   c=.3 + .16 * (hi - lo))
        if not want_nb:
            return inv
        o = dve(lambda e: e.tensor_scalar(nb[:, r, lo:hi], mv[:, r, lo:hi, 0], -1.0, None, ALU.mult), aggr, c=.07)
        o = pool(lambda e: e.tensor_tensor(nb[:, r, lo:hi], nb[:, r, lo:hi], rs[:, r, lo:hi], ALU.mult), o, inv, c=.15)
        return [inv, o]

    def back(ts, nbuf, ready, consume):
        all4 = []

        def one(m):
            bk, free = t2r.take()

            def f(e):
                for i in range(4):
                    r = e.transpose(PS[6 + bk][:, i * 128:(i + 1) * 128], ntok[nbuf][:, i, m * 128:(m + 1) * 128], ident[:])
                return r

            o = pe(f, ready, free, c_id, c=.43)
            all4.append(o)
            consume(ts[m] + .5, m, bk, o)
            if m == KC - 1:
                ntr.give(nbuf, all4)

        for m in range(KC):
            at(ts[m], lambda m=m: one(m))

    def xhat(b, K):
        s = 2 * (b % 2)
        st = {}

        def load():
            ld_x[b] = dma("d_xb", lambda e: e.dma_start(xbuf[:], x_v[b]), st_x["used"])

        def a():
            r, free = stat.take()
            st["r"] = r
            ag = []
            for i in range(4):
                o = dve(lambda e, i=i: e.bn_stats(bn[:, r, i, :], xbuf[:, i, :]), ld_x[b], free)
                ag.append(dve(lambda e, i=i: e.bn_aggr(mv[:, r, i, :], bn[:, r, i, :]), o, c=.07))
            st["inv"] = inv_std(r, 0, 4, ag, False)

        def n():
            r = st["r"]
            nbuf, free = ntr.take()
            nrm = [dve(lambda e, i=i: e.tensor_scalar(ntok[nbuf][:, i, :], xbuf[:, i, :], mv[:, r, i, 0:1], rs[:, r, i:i + 1],
                                                      ALU.subtract, ALU.mult), st["inv"], free) for i in range(4)]
            stat.give(r, nrm)
            st_x["used"] = nrm
            a_rdy[s] = None
            st["a"] = []
            back([K - 10.7, K - 10.69, K - 7.2, K - 7.19], nbuf, nrm, consume)

        def consume(t, m, bk, op):
            def h():
                hi = act(lambda e: e.activation(AH[s][:, m, :], PS[6 + bk][:], ACT.Copy), op, a_used[s])
                lo = dve(lambda e: e.tensor_tensor(AL[s][:, m, :], PS[6 + bk][:], AH[s][:, m, :].bitcast(F32),
                                                   ALU.subtract), hi)
                st["a"] += [hi, lo]
                if m == KC - 1:
                    a_rdy[s] = st["a"]
                t2r.give(bk, hi, lo)
            at(t, h)

        if b > 0:
            at(max(K - 28, -13.9), load)
        at(K - 18, a)
        at(K - 14, n)

    st_x = {"used": None}

    def tail(b, d, l, K, k1, k2):
        s = 2 * (b % 2) + d
        st = {"nrm": []}
        evs, t1s = [], []

        def t1(pr):
            if pr == 0:
                st["r"], st["free"] = stat.take()
            r = st["r"]
            got = []
            for i in (2 * pr, 2 * pr + 1):
                bk, free = t1r.take()

                def f(e, i=i, bk=bk):
                    for m in range(KC):
                        o = e.transpose(PS[2 + bk][:, m * 128:(m + 1) * 128], H[s][:, m, i * 128:(i + 1) * 128], ident[:])
                    return o

                assert len(state[(b, d, l)]) == KC
                t = pe(f, state[(b, d, l)], free, c_id, c=.43)
                got.append((i, bk, t))
                t1s.append(t)
            if pr == 1:
                h_used[s] = t1s
            at(K + k1[pr] + .5, lambda: stats(pr, got))

        def stats(pr, got):
            r = st["r"]
            ag = []
            for i, bk, t in got:
                o = dve(lambda e, i=i, bk=bk: e.bn_stats(bn[:, r, i, :], PS[2 + bk][:]), t, st["free"])
                ag.append(dve(lambda e, i=i: e.bn_aggr(mv[:, r, i, :], bn[:, r, i, :]), o, c=.07))
            inv = inv_std(r, 2 * pr, 2 * pr + 2, ag, True)
            at(K + k1[pr] + 2.9, lambda: norm(pr, got, ag, inv))

        def norm(pr, got, ag, inv):
            r = st["r"]
            if pr == 0:
                st["nt"], st["ntfree"] = ntr.take()
            for i, bk, t in got:
                o = act(lambda e, i=i, bk=bk: e.activation(ntok[st["nt"]][:, i, :], PS[2 + bk][:], ACT.Identity,
                                                           bias=nb[:, r, i:i + 1], scale=rs[:, r, i:i + 1]),
                        inv, t, ag, st["ntfree"], c=.66)
                st["nrm"].append(o)
                t1r.give(bk, o)
            if pr == 1:
                stat.give(r, *st["nrm"])
                if l < 3:
                    a_rdy[s], st["a"] = None, []
                back([K + k for k in k2], st["nt"], st["nrm"], consume)

        def consume(t, m, bk, op):
            def h():
                dst = fin if l == 3 else H[s]
                ev = act(lambda e: e.activation(dst[:, m, :], PS[6 + bk][:], ACT.Identity, bias=bet[:, m:m + 1],
                                                scale=gam[:, m:m + 1]), op, ld_g, ld_b, fin_free[0] if l == 3 else None)
                evs.append(ev)
                t2r.give(bk, ev)
                if l < 3:
                    if m % 2:
                        at(t + .8, lambda: halves(m))
                elif m == KC - 1:
                    at(t + .7, store)
            at(t, h)

        def halves(m):
            sl = slice(m - 1, m + 1)
            hi = dve(lambda e: e.tensor_copy(AH[s][:, sl, :], H[s][:, sl, :]), evs[m - 1], evs[m], a_used[s])
            lo = dve(lambda e: e.tensor_tensor(AL[s][:, sl, :], H[s][:, sl, :], AH[s][:, sl, :].bitcast(F32),
                                               ALU.subtract), hi, c=1.14)
            st["a"] += [hi, lo]
            if m == KC - 1:
                a_rdy[s], h_rdy[s] = st["a"], evs

        def store():
            st_ = [dma(f"d_xs{i}", lambda e, i=i: e.dma_start(hs[b * 4 + i, :, d, :, :], fin[:, :, i * 128:(i + 1) * 128]),
                       evs) for i in range(4)]
            fin_free[0] = st_
            hs_done[(b, d)] = st_

        at(K + k1[0], lambda: t1(0))
        at(K + k1[1], lambda: t1(1))

    state = {}

    def job(b, d, l):
        s = 2 * (b % 2) + d
        K = base[(b, d, l)]
        mms = []
        if l == 0:
            state[(b, 0, 0)], state[(b, 1, 0)] = [], []
        else:
            state[(b, d, l)] = []

        def mm(m):
            bk, free = gate.take()

            def f(e):
                steps = [(w, a, k) for k in range(KC) for w, a in ((WH[l], AH[s]), (WH[l], AL[s]), (WL[l], AH[s]))]
                for j, (w, a, k) in enumerate(steps):
                    r = e.matmul(PS[bk][:], w[:, k, m * 128:(m + 1) * 128], a[:, k, :], start=(j == 0),
                                 stop=(j == len(steps) - 1))
                return r

            assert a_rdy[s] and w_rdy[l], "operands are not planned yet"
            o = pe(f, a_rdy[s], w_rdy[l], free, c=2.57)
            mms.append(o)
            if m == KC - 1:
                a_used[s] = mm_done[(b, d, l)] = mms
            at(K + 3.5 * m + 2.6, lambda: gates(m, bk, o))

        def gates(m, bk, o):
            c, free = chr_.take()
            t = K + 3.5 * m + 2.6
            sg = act(lambda e: e.activation(zb[c][:], PS[bk][:], ACT.Sigmoid, bias=condt[:, l, m:m + 1]), o, free, ld_c)
            tn = act(lambda e: e.activation(hb[c][:], PS[bk][:], ACT.Tanh, bias=condt[:, l, m:m + 1]), o, free, ld_c)
            gate.give(bk, sg, tn)
            at(t + .7, lambda: keep(m, c, sg, tn))

        def keep(m, c, sg, tn):
            t = K + 3.5 * m + 2.6
            aa = dve(lambda e: e.scalar_tensor_tensor(ab[c][:], zb[c][:], 1.0, tiny[:, 0:1].broadcast_to([128, S]),
                                                      ALU.subtract, ALU.max, reverse0=True), sg, c_tiny)
            vv = pool(lambda e: e.tensor_tensor(hb[c][:], zb[c][:], hb[c][:], ALU.mult), sg, tn)
            at(t + 2.6, lambda: scan(m, c, aa, vv))

        def scan(m, c, aa, vv):
            t = K + 3.5 * m + 2.6
            if l == 0:
                both = []
                for dd in range(2):
                    tgt = 2 * (b % 2) + dd
                    rv = slice(None, None, -1) if dd else slice(None)
                    sc = dve(lambda e, tgt=tgt, rv=rv: e.tensor_tensor_scan(H[tgt][:, m, :][:, rv], ab[c][:, rv], hb[c][:, rv],
                                                                            0.0, ALU.mult, ALU.add), aa, vv, h_used[tgt])
                    state[(b, dd, 0)].append(sc)
                    both.append(sc)
                chr_.give(c, both)
                return
            rv = slice(None, None, -1) if d else slice(None)
            sc = dve(lambda e: e.tensor_tensor_scan(zb[c][:, rv], ab[c][:, rv], hb[c][:, rv], 0.0, ALU.mult, ALU.add), aa, vv)
            at(t + 3.3, lambda: resid(m, c, sc))

        def resid(m, c, sc):
            r = pool(lambda e: e.tensor_tensor(H[s][:, m, :], H[s][:, m, :], zb[c][:], ALU.add), sc, h_rdy[s], a_rdy[s])
            state[(b, d, l)].append(r)
            chr_.give(c, r)

        for m in range(KC):
            at(K + 3.5 * m, lambda m=m: mm(m))
        if l == 0:
            tail(b, 0, 0, K, [16.7, 20.2], [24.6, 24.7, 25.6, 25.7])
            tail(b, 1, 0, K, [23.7, 27.2], [30.7, 30.8, 34.1, 34.2])
        else:
            tail(b, d, l, K, [20.2, 23.7], [30.65, 30.66, 34.05, 34.06])

    for j in jobs:
        if j[2] == 0:
            xhat(j[0], base[j])
        job(*j)

    pieces = [(0, k, c) for k in range(4) for c in range(4)] + [(1, k, 0) for k in range(16)]

    def src(w, k, c):
        return fct_v[:, k, c, :] if w == 0 else pjt_v[:, k, :]

    sums = []
    stg_free = [None]

    def abs_load(n):
        w, k, c = pieces[n]
        ld = dma("d_st4", lambda e: e.dma_start(stg[:], src(w, k, c)), stg_free[0])
        at(38 + n * 10.0, lambda: abs_sum(n, ld))

    def abs_sum(n, ld):
        a = act(lambda e: e.activation(stg[:], stg[:], ACT.Abs, accum_out=asum[:, n:n + 1]), ld)
        sums.append(a)
        stg_free[0] = [a]

    for n in range(32):
        at(32 + n * 10.0, lambda n=n: abs_load(n))

    thr = []

    def totals():
        r = [dve(lambda e, w=w: e.reduce_sum(ssum[:, w:w + 1], asum[:, 16 * w:16 * w + 16], axis=AX_X), sums) for w in range(2)]
        t = pool(lambda e: e.partition_all_reduce(tot[:], ssum[:], 128, RADD), r)
        o = dve(lambda e: e.tensor_scalar(th[:], tot[:], 1.0 / (512 * HID), 1e-6, ALU.mult, ALU.add), t)
        o1 = dve(lambda e: e.tensor_scalar(nth[:], th[:], -0.5, None, ALU.mult), o)
        o2 = dve(lambda e: e.tensor_scalar(th[:], th[:], 0.5, None, ALU.mult), o1)
        thr.extend([o1, o2])

    at(380, totals)

    srcb = Ring(5)
    sbuf5 = [xbuf[:, i, :] for i in range(4)] + [stg[:]]
    fu_rdy, fc_rdy, pj_rdy = [], [], []

    def prep(t, ap, free_ops, work):
        def ld():
            i, free = srcb.take()
            w = [free if free is not None else [st_x["used"], sums]]
            o = dma(f"d_st{i}", lambda e: e.dma_start(sbuf5[i], ap), *w)
            at(t, lambda: go(i, o))

        def go(i, o):
            last = work(sbuf5[i], o, free_ops())
            srcb.give(i, last)

        at(t - 5, ld)

    def fuse_w(k):
        def work(buf, ld, free):
            hi = dve(lambda e: e.tensor_copy(FUH[:, k, :], buf), ld, free)
            lo = dve(lambda e: e.tensor_tensor(FUL[:, k, :], buf, FUH[:, k, :].bitcast(F32), ALU.subtract), hi)
            fu_rdy.extend([hi, lo])
            return lo
        return work

    def ternary(w, dst, rdy):
        def work(buf, ld, free):
            a = dve(lambda e: e.tensor_scalar(dst, buf, th[:, w:w + 1], None, ALU.is_gt), ld, free, thr)
            o = dve(lambda e: e.scalar_tensor_tensor(dst, buf, nth[:, w:w + 1], dst.bitcast(F32), ALU.is_lt, ALU.subtract,
                                                     reverse1=True), a)
            rdy.append(o)
            return o
        return work

    of_layer = lambda l: [mm_done[(b, d, l)] for b in (NB - 2, NB - 1) for d in range(2)]
    for k in range(8):
        prep(END - 8 * T + 8 + 5.0 * k, fwt_v[:, k, :], lambda: of_layer(1), fuse_w(k))
    for k in range(2):
        for c in range(4):
            prep(END - 4 * T + 4 + 3.0 * (4 * k + c), fct_v[:, k, c, :], lambda: of_layer(2),
                 ternary(0, FCA[:, k, c * 512:(c + 1) * 512], fc_rdy))
    for k in range(16):
        prep(END - 2 * T + 4 + 1.8 * k, pjt_v[:, k, :], lambda: [a_used[0], a_used[1]],
             ternary(1, PJ[:, k, :], pj_rdy))
    for k in range(2):
        for c in range(4):
            prep(END + 8 + 1.5 * (4 * k + c), fct_v[:, 2 + k, c, :], lambda: a_used[2],
                 ternary(0, FCB[:, k, c * 512:(c + 1) * 512], fc_rdy))

    NU = NB * 4
    V0 = END + U + 4
    over = lambda ring, *idx: [lambda i=i: ring.free[i] for i in idx]
    hcr = Ring(2, [lambda: a_used[3]] * 2)
    xrr = Ring(2, [lambda: a_used[3]] * 2)
    hlr = Ring(2, [lambda: of_layer(3)] * 2)
    x1r = Ring(3, over(chr_, 0, 1, 0))
    n1r = Ring(2, over(chr_, 1, 0))
    xhr = Ring(2, [lambda: h_used[0]] * 2)
    ur = Ring(4, [lambda: [h_used[2], h_used[3]]] * 4)
    gr = Ring(2, over(ntr, 0, 1))
    obr = Ring(2, [lambda: fin_free[0]] * 2)
    fubank = Ring(1, over(gate, 0))
    t1bank = Ring(1, over(gate, 1))
    pjbank = Ring(1, over(t1r, 0))
    fcbank = Ring(2, over(t1r, 1, 2))
    t2bank = Ring(3, over(t1r, 3) + over(t2r, 0, 1))
    rows = {}
    outs = []

    def load_rows():
        rows["fbb"] = dma("d_fb", lambda e: e.dma_start(fbb[:], fb.partition_broadcast(128)), chr_.free[1])
        rows["w"] = dma("d_row", lambda e: e.dma_start(wrow[:], lnw.partition_broadcast(128)), h_used[1], c=5)

    at(END + 4, load_rows)

    def load_b():
        rows["b"] = dma("d_lnb", lambda e: e.dma_start(lnbt[:], lnb), fin_free[0])

    at(END + 34, load_b)

    def bias_row():
        bk, free = pjbank.take()
        ring = Ring(2, [fin_free[0]] * 2)
        m = None
        for k in range(16):
            i, fr = ring.take()
            hi = dve(lambda e, k=k, i=i: e.tensor_copy(bh[i][:, 0, :], lnbt[:, k:k + 1].broadcast_to([128, 128])), rows["b"],
                     fr, c=.2)
            lo = dve(lambda e, k=k, i=i: e.tensor_tensor(bh[i][:, 1, :], lnbt[:, k:k + 1].broadcast_to([128, 128]),
                                                         bh[i][:, 0, :].bitcast(F32), ALU.subtract), hi, c=.2)

            def f(e, k=k, i=i):
                e.matmul(PS[2][:], bh[i][:, 0, :], PJ[:, k, :], start=(k == 0), stop=False)
                return e.matmul(PS[2][:], bh[i][:, 1, :], PJ[:, k, :], start=False, stop=(k == 15))

            m = pe(f, hi, lo, pj_rdy, free, after=m, c=.43)
            ring.give(i, m)
        o = act(lambda e: e.activation(cB[:], PS[2][:], ACT.Copy), m, fin_free[0])
        rows["cB"] = o
        pjbank.give(bk, o)

    at(END + 44, bias_row)

    def unit(u):
        V = V0 + U * u
        b = u // 4
        st = {}
        fcs, t2s = [], []

        def load():
            i, free = hcr.take()
            st["hc"] = i
            st["ld"] = dma(f"d_hc{i}", lambda e: e.dma_start(hc[i][:], hs[u].rearrange("p d m t -> p (d m) t")), free,
                           hs_done[(b, 0)], hs_done[(b, 1)])
            i2, free = xrr.take()
            st["xr"] = i2
            st["ldx"] = dma(f"d_x{i2}", lambda e: e.dma_start(xr[i2][:], x[b, (u % 4) * 128:(u % 4 + 1) * 128, :]), free)

        def split():
            i, free = hlr.take()
            st["hl"] = i
            hi = dve(lambda e: e.tensor_copy(hch[i][:], hc[st["hc"]][:]), st["ld"], free)
            lo = dve(lambda e: e.tensor_tensor(hcl[i][:], hc[st["hc"]][:], hch[i][:].bitcast(F32), ALU.subtract), hi, c=1.14)
            hcr.give(st["hc"], lo)
            st["split"] = [hi, lo]

        def addx():
            j = st["xr"]
            st["xf"] = pool(lambda e: e.tensor_tensor(xf[j][:], xr[j][:], fbb[:], ALU.add), st["ldx"], rows["fbb"], free_xf[j])

        def fuse():
            bk, free = fubank.take()
            i = st["hl"]

            def f(e):
                n = 0
                for k in range(8):
                    for a, w in ((hch, FUH), (hch, FUL), (hcl, FUH)):
                        r = e.matmul(PS[0][:], a[i][:, k, :], w[:, k, :], start=(n == 0), stop=(n == 23))
                        n += 1
                return r

            o = pe(f, st["split"], fu_rdy, free, c=5.13)
            hlr.give(i, o)
            st["fuse"] = o

        def resid():
            i, free = x1r.take()
            st["x1"] = i
            j = st["xr"]
            o = dve(lambda e: e.tensor_tensor(x1[i][:], PS[0][:], xf[j][:], ALU.add), st["fuse"], st["xf"], free)
            fubank.give(0, o)
            free_xf[j] = o
            xrr.give(j, st["xf"])
            r, free = stat.take()
            st["r1"] = r
            o = dve(lambda e: e.bn_stats(bn[:, r, 0, :], x1[i][:]), o, free)
            o = dve(lambda e: e.bn_aggr(mv[:, r, 0, :], bn[:, r, 0, :]), o)
            st["inv1"] = inv_std(r, 0, 1, [o], False)

        def norm():
            i, r = st["x1"], st["r1"]
            j, free = n1r.take()
            st["n1"] = j
            st["nrm"] = dve(lambda e: e.tensor_scalar(n1[j][:], x1[i][:], mv[:, r, 0, 0:1], rs[:, r, 0:1], ALU.subtract,
                                                      ALU.mult), st["inv1"], free, c=.33)
            stat.give(r, st["nrm"])

        def t1():
            bk, free = t1bank.take()
            j = st["n1"]

            def f(e):
                for m in range(4):
                    o = e.transpose(PS[1][:, m * 128:(m + 1) * 128], n1[j][:, m * 128:(m + 1) * 128], ident[:])
                return o

            o = pe(f, st["nrm"], free, c=.43)
            n1r.give(j, o)
            st["t1"] = o

        def t1out():
            i, free = xhr.take()
            st["xh"] = i
            hi = act(lambda e: e.activation(xh[i][:].rearrange("p a t -> p (a t)"), PS[1][:], ACT.Copy), st["t1"], free, c=.48)
            lo = dve(lambda e: e.tensor_tensor(xl[i][:].rearrange("p a t -> p (a t)"), PS[1][:],
                                               xh[i][:].rearrange("p a t -> p (a t)").bitcast(F32), ALU.subtract), hi)
            t1bank.give(0, hi, lo)
            st["xhl"] = [hi, lo]

        def addc():
            i = st["x1"]
            st["xc"] = pool(lambda e: e.tensor_tensor(x1[i][:], x1[i][:], cB[:], ALU.add), st["nrm"], rows["cB"])

        def fc(n):
            bk, free = fcbank.take()
            i = st["xh"]

            def f(e):
                c = 0
                for k in range(4):
                    wk = FCA[:, k, n * 512:(n + 1) * 512] if k < 2 else FCB[:, k - 2, n * 512:(n + 1) * 512]
                    for a in (xh, xl):
                        r = e.matmul(PS[3 + bk][:], a[i][:, k, :], wk, start=(c == 0), stop=(c == 7))
                        c += 1
                return r

            o = pe(f, st["xhl"], fc_rdy, free, c=1.71)
            fcs.append(o)
            if n == 3:
                xhr.give(i, fcs)
            at(V + 5.1 + 1.7 * n + 1.75, lambda: gelu(n, bk, o))

        def gelu(n, bk, o):
            if n == 0:
                st["g"], st["gfree"] = gr.take()
                st["r2"], st["sfree"] = stat.take()
                st["bn"] = []
            i, r = st["g"], st["r2"]
            a = act(lambda e: e.activation(g[i][:, n * 512:(n + 1) * 512], PS[3 + bk][:], ACT.Gelu), o, st["gfree"], c=.48)
            fcbank.give(bk, a)
            st["bn"].append(dve(lambda e: e.bn_stats(bn[:, r, n, :], g[i][:, n * 512:(n + 1) * 512]), a, st["sfree"]))
            if n == 3:
                o = dve(lambda e: e.bn_aggr(mv[:, r, 0, :], bn[:, r, :, :]), st["bn"])
                st["ag2"] = o
                st["inv2"] = inv_std(r, 0, 1, [o], False)

        def scale(n):
            i, r = st["g"], st["r2"]
            sl = slice(n * 512, (n + 1) * 512)
            o = dve(lambda e: e.scalar_tensor_tensor(g[i][:, sl], g[i][:, sl], mv[:, r, 0, 0:1], wrow[:, sl],
                                                     ALU.subtract, ALU.mult), st["ag2"], st["bn"], rows["w"])
            st.setdefault("sc", []).append(o)

        def t2(n):
            bk, free = t2bank.take()
            i = st["g"]

            def f(e):
                for m in range(4):
                    c = n * 512 + m * 128
                    o = e.transpose(PS[5 + bk][:, m * 128:(m + 1) * 128], g[i][:, c:c + 128], ident[:])
                return o

            o = pe(f, st["sc"][n], free, c=.43)
            t2s.append(o)
            if n == 3:
                gr.give(i, t2s)
            at(t2k[n] + V + .3, lambda: t2out(n, bk, o))

        def t2out(n, bk, o):
            j, free = ur.take()
            hi = act(lambda e: e.activation(uth[j][:].rearrange("p a t -> p (a t)"), PS[5 + bk][:], ACT.Copy), o, free, c=.48)
            lo = dve(lambda e: e.tensor_tensor(utl[j][:].rearrange("p a t -> p (a t)"), PS[5 + bk][:],
                                               uth[j][:].rearrange("p a t -> p (a t)").bitcast(F32), ALU.subtract), hi)
            t2bank.give(bk, hi, lo)
            st[("ut", n)] = (j, [hi, lo])

        def proj(n):
            if n == 0:
                bk, st["pfree"] = pjbank.take()
            j, rdy = st[("ut", n)]

            def f(e):
                for m in range(4):
                    for a in (uth, utl):
                        r = e.matmul(PS[2][:], a[j][:, m, :], PJ[:, 4 * n + m, :], start=(n == 0 and m == 0 and a is uth),
                                     stop=(n == 3 and m == 3 and a is utl))
                return r

            o = pe(f, rdy, pj_rdy, st["pfree"], after=st.get("pj"), c=1.71)
            ur.give(j, o)
            st["pj"] = o

        def final():
            i, free = obr.take()
            r, k = st["r2"], st["x1"]
            o = dve(lambda e: e.scalar_tensor_tensor(ob[i][:], PS[2][:], rs[:, r, 0:1], x1[k][:], ALU.mult, ALU.add),
                    st["pj"], st["inv2"], st["xc"], free)
            pjbank.give(0, o)
            stat.give(r, o)
            x1r.give(k, o)
            d = dma(f"d_o{i}", lambda e: e.dma_start(out[b, (u % 4) * 128:(u % 4 + 1) * 128, :], ob[i][:]), o)
            obr.give(i, d)
            outs.append(d)

        t2k = [25.0, 25.05, 32.0, 33.7]
        pjk = [32.1, 33.8, 35.5, 37.2]
        at(max(V - 32, END + .5 + .01 * u), load)
        at(max(V - 26, END + 2), split)
        at(V - 20, fuse)
        at(V - 17, addx)
        at(V - 14.8, resid)
        at(V - 11, norm)
        at(V - 8, t1)
        at(V - 7.6, t1out)
        at(V - 2, addc) if u > 1 else at(END + 60 + u, addc)
        for n in range(4):
            at(V + 5.1 + 1.7 * n, lambda n=n: fc(n))
            at(V + 14.5 + .6 * n, lambda n=n: scale(n))
            at(V + t2k[n], lambda n=n: t2(n))
            at(V + pjk[n], lambda n=n: proj(n))
        at(V + 39.2, final)

    free_xf = [None, None]
    for u in range(NU):
        unit(u)

    while plan:
        plan.sort(key=lambda p: p[:2])
        t, _, step = plan.pop()
        now[0] = -t
        step()
    q.arrange()

    totals_ = q.count()
    sems = {n: ctx.enter_context(nc.semaphore("s_" + n)) for n in totals_}
    block = ctx.enter_context(nc.Block())

    @block.tensor
    def _(e):
        q.emit("pe", e, sems)

    @block.scalar
    def _(e):
        q.emit("act", e, sems)

    @block.vector
    def _(e):
        q.emit("dve", e, sems)

    @block.gpsimd
    def _(e):
        q.emit("pool", e, sems)

    @block.sync
    def _(e):
        q.emit("sp", e, sems)
        for name, value in totals_.items():
            if name.startswith("d_"):
                e.wait_ge(sems[name], value)

    ctx.close()


def kernel(**inputs):
    import numpy as _np
    import concourse.bacc as _bacc
    from concourse import mybir as _mybir
    from concourse.bass_utils import run_bass_kernel_spmd as _run

    a = {k: _np.asarray(v) for k, v in inputs.items()}
    cols = lambda v: v.reshape(-1, 128).T
    data = {
        "x": a["x"],
        "wt": a["ctx_1024"][:L].transpose(0, 2, 1),
        "cond": a["cond_1024"][:L].reshape(L, KC, 128).transpose(2, 0, 1),
        "fwt": a["L0_xcond_fusion_W"].T,
        "fb": a["L0_xcond_fusion_b"],
        "gamma": cols(a["L0_xcond_ln_gamma"]),
        "beta": cols(a["L0_xcond_ln_beta"]),
        "fct": a["L0_ffn_W_fc"].T,
        "lnw": a["L0_ffn_ln_w"],
        "lnb": cols(a["L0_ffn_ln_b"]),
        "pjt": a["L0_ffn_W_proj"].T,
    }
    nc = _bacc.Bacc("TRN2", target_bir_lowering=False, num_devices=1)
    arrays, args = {}, []
    for name, v in data.items():
        v = _np.ascontiguousarray(v)
        arrays[f"in_{name}"] = v
        args.append(nc.dram_tensor(f"in_{name}", v.shape, _mybir.dt.from_np(v.dtype), kind="ExternalInput").ap())
    o = nc.dram_tensor("out_0", (NB, S, 512), _mybir.dt.float32, kind="ExternalOutput").ap()
    pixart_block(nc, *args, o)
    r = _run(nc, [arrays], core_ids=[0])
    return r.results[0]["out_0"]
```

```python
from contextlib import ExitStack

import concourse.bass as bass
from concourse import mybir

F32 = mybir.dt.float32
F32R = mybir.dt.float32r
ALU = mybir.AluOpType
ACT = mybir.ActivationFunctionType
AX_X = mybir.AxisListType.X
RADD = bass.bass_isa.ReduceOp.add

NB = 8
S = 512
HID = 2048
L = 4
KC = 4
EPS = 1e-5
U = 21.0
T = 14.266
CHUNK = 3.464
TOK = [20.009, 23.182]
BACK = [30.938, 31.407, 34.385, 34.389]
TOK_F0 = [17.156, 19.883]
BACK_F0 = [24.188, 26.64, 26.736, 27.41]
TOK_B0 = [23.399, 27.957]
BACK_B0 = [29.752, 30.793, 33.355, 35.788]
XHAT_BACK = [-9.238, -9.033, -6.826, -6.557]
XHAT_AT = [-16.1, -16.053]
HALVES = 0.562
NORM = 3.282
GATES = 1.92
KEEP = 1.216
SCAN = 2.909
RESID = 3.104
PREP = [1.023, 5.066, 1.559, 3.011, 0.811, 2.14, 1.749, 1.812]
SPLIT = [10.0, 30.0, 50.0, 2.0]
START2 = 17.92
CB_AT = 37.04
JOBS = [
    (0, 0, 0), (1, 0, 0), (0, 0, 1), (0, 1, 1), (1, 0, 1), (0, 0, 2), (0, 1, 2),
    (1, 1, 1), (0, 0, 3), (0, 1, 3), (1, 1, 2), (1, 0, 2), (2, 0, 0), (1, 1, 3),
    (1, 0, 3), (2, 0, 1), (2, 1, 1), (3, 0, 0), (2, 0, 2), (2, 1, 2), (3, 0, 1),
    (3, 1, 1), (2, 1, 3), (2, 0, 3), (3, 1, 2), (3, 0, 2), (4, 0, 0), (3, 1, 3),
    (3, 0, 3), (4, 0, 1), (4, 1, 1), (5, 0, 0), (4, 0, 2), (4, 1, 2), (5, 0, 1),
    (5, 1, 1), (4, 0, 3), (4, 1, 3), (5, 0, 2), (5, 1, 2), (6, 0, 0), (5, 0, 3),
    (5, 1, 3), (6, 1, 1), (6, 0, 1), (7, 0, 0), (6, 1, 2), (6, 0, 2), (7, 1, 1),
    (7, 0, 1), (6, 1, 3), (7, 1, 2), (7, 0, 2), (6, 0, 3), (7, 1, 3), (7, 0, 3),
]


class Op:

    def __init__(self, eng, fn, waits, after, sem, key, cost):
        self.eng, self.fn, self.waits, self.after, self.sem = eng, fn, waits, after, sem
        self.key, self.cost = key, cost
        self.at = None
        self.used = False


def flatten(w):
    if w is None:
        return []
    if isinstance(w, (list, tuple)):
        return [o for x in w for o in flatten(x)]
    return [w]


class Queues:

    SLACK = {"pe": 0.127, "act": 0.075, "dve": 0.104, "pool": 0.331, "sp": 0.}
    REACH = {"pe": .2, "act": .15, "dve": .13, "pool": .13, "sp": 2.}

    def __init__(self, engines):
        self.ops = []
        self.order = {e: [] for e in engines}

    def add(self, eng, fn, waits, key, cost, sem=None, after=None):
        waits, after = flatten(waits), flatten(after)
        for o in waits:
            o.used = True
        op = Op(eng, fn, waits, after, sem, key, cost)
        self.ops.append(op)
        return op

    def arrange(self):
        left, users, ready = {}, {}, {e: [] for e in self.order}
        done = {}
        for n, o in enumerate(self.ops):
            o.n = n
            deps = {id(w): w for w in o.waits + o.after}
            left[o] = len(deps)
            for w in deps.values():
                users.setdefault(w, []).append(o)
            if not deps:
                ready[o.eng].append((0., o))
        free = {e: 0. for e in self.order}
        for _ in range(len(self.ops)):
            best = None
            for e, c in ready.items():
                if c:
                    start = min(max(free[e], t) for t, _ in c)
                    if best is None or start < best[0]:
                        best = (start, e)
            start, e = best
            limit = start + self.SLACK[e]
            t, o = min((x for x in ready[e] if max(free[e], x[0]) <= limit), key=lambda x: (x[1].key, x[1].n))
            ready[e].remove((t, o))
            begin = max(free[e], t)
            hold = .08 if e == "sp" else o.cost
            free[e] = begin + hold
            done[o] = begin + o.cost + self.REACH[e]
            self.order[e].append(o)
            for u in users.get(o, []):
                left[u] -= 1
                if not left[u]:
                    same = [begin + o.cost if w.eng == u.eng == "pe" else done[w] for w in u.waits]
                    ready[u.eng].append((max([0.] + same), u))

    def count(self):
        total = {}
        for eng, ops in self.order.items():
            for o in ops:
                if o.used or o.sem:
                    name = o.sem or eng
                    total[name] = total.get(name, 0) + (16 if o.sem else 1)
                    o.at = (name, total[name])
        return total

    def emit(self, eng, e, sems):
        seen = {}
        for o in self.order[eng]:
            need = {}
            for w in o.waits:
                name, value = w.at
                need[name] = max(need.get(name, 0), value)
            for name, value in need.items():
                if seen.get(name, 0) < value:
                    e.wait_ge(sems[name], value)
                    seen[name] = value
            last = o.fn(e)
            if o.at:
                last.then_inc(sems[o.at[0]], 16 if o.sem else 1)


class Ring:

    def __init__(self, n, first=None):
        self.n, self.i = n, 0
        self.free = list(first) if first else [None] * n

    def take(self):
        i = self.i % self.n
        self.i += 1
        w = self.free[i]() if callable(self.free[i]) else self.free[i]
        assert w != "held", "a buffer is taken before its release is planned"
        self.free[i] = "held"
        return i, w

    def give(self, i, *ops):
        self.free[i] = list(ops)


def pixart_block(nc, x, wt, cond, fwt, fb, gamma, beta, fct, lnw, lnb, pjt, out):
    hs = nc.dram_tensor("hs_scratch", [NB, 128, 2 * KC, S], F32, kind="Internal").ap()
    q = Queues(["pe", "act", "dve", "pool", "sp"])
    ctx, p0, p1, p2 = ExitStack(), ExitStack(), ExitStack(), ExitStack()

    def sb(stack, name, shape, dt=F32):
        return stack.enter_context(nc.sbuf_tensor(name, shape, dt))

    now = [-30.]

    def pe(fn, *w, c=2.6, after=None):
        return q.add("pe", fn, w, now[0], c, after=after)

    def act(fn, *w, c=.57):
        return q.add("act", fn, w, now[0], c)

    def dve(fn, *w, c=.6):
        return q.add("dve", fn, w, now[0], c)

    def pool(fn, *w, c=1.23):
        return q.add("pool", fn, w, now[0], c)

    def dma(sem, fn, *w, c=3.):
        return q.add("sp", fn, w, now[0], c, sem=sem)

    plan = []
    made = [0]

    def at(t, fn):
        made[0] += 1
        plan.append((-t, -made[0], fn))

    ident = sb(ctx, "ident", [128, 128])
    nhalf = sb(ctx, "nhalf", [128, 4])
    tiny = sb(ctx, "tiny", [128, 1])
    condt = sb(ctx, "condt", [128, L, KC])
    gam = sb(ctx, "gam", [128, KC])
    bet = sb(ctx, "bet", [128, KC])
    asum = sb(ctx, "asum", [128, 32])
    ssum = sb(ctx, "ssum", [128, 2])
    tot = sb(ctx, "tot", [128, 2])
    th = sb(ctx, "th", [128, 2])
    nth = sb(ctx, "nth", [128, 2])
    NST = 4
    bn = sb(ctx, "bn", [128, NST, 4, 6])
    mv = sb(ctx, "mv", [128, NST, 4, 2])
    ve = sb(ctx, "ve", [128, NST, 4])
    rs = sb(ctx, "rs", [128, NST, 4])
    nb = sb(ctx, "nb", [128, NST, 4])
    stg = sb(ctx, "stg", [128, 512])
    xbuf = sb(ctx, "xbuf", [128, 4, 512])

    RAW = []
    for l in range(L):
        sb(p0, f"gap{l}", [128, KC, 512])
        RAW.append(sb(p0, f"RAW{l}", [128, KC, 512]))
    p0.close()

    WH, WL = [], []
    for l in range(L):
        WH.append(sb(p1, f"WH{l}", [128, KC, 512], F32R))
        WL.append(sb(p1, f"WL{l}", [128, KC, 512], F32R))
    AH, AL = {}, {}
    for s in (0, 1, 3, 2):
        AH[s] = sb(p1, f"AH{s}", [128, KC, S], F32R)
        AL[s] = sb(p1, f"AL{s}", [128, KC, S], F32R)
    H = [sb(p1, f"H{s}", [128, KC, S]) for s in range(4)]
    ntok = [sb(p1, f"ntok{i}", [128, 4, 512]) for i in range(2)]
    zb = [sb(p1, f"zb{i}", [128, S]) for i in range(3)]
    hb = [sb(p1, f"hb{i}", [128, S]) for i in range(3)]
    ab = [sb(p1, f"ab{i}", [128, S]) for i in range(3)]
    p1.close()

    FUH = sb(p2, "FUH", [128, 8, 512], F32R)
    FUL = sb(p2, "FUL", [128, 8, 512], F32R)
    FCA = sb(p2, "FCA", [128, 2, HID], F32R)
    PJA = sb(p2, "PJA", [128, 8, 512], F32R)
    hch = [sb(p2, f"hch{i}", [128, 8, 128], F32R) for i in range(2)]
    hcl = [sb(p2, f"hcl{i}", [128, 8, 128], F32R) for i in range(2)]
    hc = [sb(p2, f"hc{i}", [128, 8, 128]) for i in range(2)]
    xr = [sb(p2, f"xr{i}", [128, 512]) for i in range(2)]
    xf = [sb(p2, f"xf{i}", [128, 512]) for i in range(2)]
    FCB = sb(p2, "FCB", [128, 2, HID], F32R)
    PJB = sb(p2, "PJB", [128, 8, 512], F32R)
    xh = [sb(p2, f"xh{i}", [128, 4, 128], F32R) for i in range(2)]
    xl = [sb(p2, f"xl{i}", [128, 4, 128], F32R) for i in range(2)]
    wrow = sb(p2, "wrow", [128, HID])
    uth = [sb(p2, f"uth{i}", [128, 4, 128], F32R) for i in range(4)]
    utl = [sb(p2, f"utl{i}", [128, 4, 128], F32R) for i in range(4)]
    g = [sb(p2, f"g{i}", [128, HID]) for i in range(2)]
    x1 = [sb(p2, f"x1{i}", [128, 512]) for i in range(3)]
    n10 = sb(p2, "n10", [128, 512])
    bh = [sb(p2, f"bh{i}", [128, 2, 128], F32R) for i in range(2)]
    n1 = [sb(p2, "n11", [128, 512]), n10]
    ob = [sb(p2, f"ob{i}", [128, 512]) for i in range(2)]
    cB = sb(p2, "cB", [128, 512])
    lnbt = sb(p2, "lnbt", [128, 16])
    fbb = sb(p2, "fbb", [128, 512])
    x1 = [x1[2], x1[0], x1[1]]
    PJ = [PJA[:, k, :] for k in range(8)] + [PJB[:, k, :] for k in range(8)]
    p2.close()

    PS = [ctx.enter_context(nc.psum_tensor(f"ps{i}", [128, 512], F32)) for i in range(8)]

    c_id0 = pool(lambda e: e.memset(ident[:], 0.0))
    c_id = pool(lambda e: e.affine_select(out=ident[:], in_=ident[:], compare_op=ALU.not_equal, fill=1.0,
                                          base=0, pattern=[[-1, 128]], channel_multiplier=1), c_id0)
    c_nh = pool(lambda e: e.memset(nhalf[:], -0.5))
    c_tiny = pool(lambda e: e.memset(tiny[:], 1e-8))

    x_v = x.rearrange("b (i p) d -> b p i d", p=128)
    fct_v = fct.rearrange("(k p) (c n) -> p k c n", p=128, n=512)
    pjt_v = pjt.rearrange("(k p) n -> p k n", p=128)
    fwt_v = fwt.rearrange("(k p) n -> p k n", p=128)

    jobs = JOBS
    base = {j: T * k for k, j in enumerate(jobs)}
    END = T * len(jobs)

    gate = Ring(2)
    t1r = Ring(4)
    t2r = Ring(2)
    stat = Ring(NST)
    ntr = Ring(2)
    chr_ = Ring(3)
    a_rdy, h_rdy = [None] * 4, [None] * 4
    a_used, h_used = [None] * 4, [None] * 4
    mm_done = {}
    hs_done = {}

    ld_x = {0: [dma(f"d_x0{i}", lambda e, i=i: e.dma_start(xbuf[:, i, :], x_v[0, :, i, :]), c=2.4 + .7 * i) for i in range(4)]}
    w_rdy = [None] * L

    def load_w(l, *w):
        v = wt[l].rearrange("(k p) n -> p k n", p=128)
        return [dma(f"d_w{l}{k}", lambda e, k=k: e.dma_start(RAW[l][:, k, :], v[:, k, :]), *w, c=6 if l == 0 else 4)
                for k in range(KC)]

    def split_w(l, ld, k):
        hi = act(lambda e: e.activation(WH[l][:, k, :], RAW[l][:, k, :], ACT.Copy), ld[k], c=.48)
        eng, c = (dve, .6) if l == 0 and k > 1 else (pool, 1.23)
        lo = eng(lambda e: e.tensor_tensor(WL[l][:, k, :], RAW[l][:, k, :], WH[l][:, k, :].bitcast(F32),
                                           ALU.subtract), hi, c=c)
        w_rdy[l] = (w_rdy[l] or []) + [hi, lo]
        if k == KC - 1 and l < L - 1:
            nxt = load_w(l + 1, lo)
            for kk in range(KC):
                at(SPLIT[l] + SPLIT[3] * kk, lambda kk=kk: split_w(l + 1, nxt, kk))

    ld0 = load_w(0)
    ld_c = dma("d_c0", lambda e: e.dma_start(condt[:], cond))
    ld_g = dma("d_c1", lambda e: e.dma_start(gam[:], gamma))
    ld_b = dma("d_c2", lambda e: e.dma_start(bet[:], beta))
    for k in range(KC):
        at(-16 + .1 * k, lambda k=k: split_w(0, ld0, k))

    def inv_std(r, lo, hi, aggr, want_nb):
        o = dve(lambda e: e.tensor_scalar(ve[:, r, lo:hi], mv[:, r, lo:hi, 1], EPS, None, ALU.add), aggr, c=.07)
        inv = pool(lambda e: e.tensor_tensor(rs[:, r, lo:hi], ve[:, r, lo:hi], nhalf[:, lo:hi], ALU.pow), o, c_nh,
                   c=.3 + .16 * (hi - lo))
        if not want_nb:
            return inv
        o = dve(lambda e: e.tensor_scalar(nb[:, r, lo:hi], mv[:, r, lo:hi, 0], -1.0, None, ALU.mult), aggr, c=.07)
        o = pool(lambda e: e.tensor_tensor(nb[:, r, lo:hi], nb[:, r, lo:hi], rs[:, r, lo:hi], ALU.mult), o, inv, c=.15)
        return [inv, o]

    def back(ts, nbuf, ready, consume):
        all4 = []

        def one(m):
            bk, free = t2r.take()

            def f(e):
                for i in range(4):
                    r = e.transpose(PS[6 + bk][:, i * 128:(i + 1) * 128], ntok[nbuf][:, i, m * 128:(m + 1) * 128], ident[:])
                return r

            o = pe(f, ready, free, c_id, c=.43)
            all4.append(o)
            consume(ts[m] + .5, m, bk, o)
            if m == KC - 1:
                ntr.give(nbuf, all4)

        for m in range(KC):
            at(ts[m], lambda m=m: one(m))

    def xhat(b, K):
        s = 2 * (b % 2)
        st = {}

        def load():
            ld_x[b] = dma("d_xb", lambda e: e.dma_start(xbuf[:], x_v[b]), st_x["used"])
            st_x["used"] = "held"

        def a():
            r, free = stat.take()
            st["r"] = r
            ag = []
            for i in range(4):
                o = dve(lambda e, i=i: e.bn_stats(bn[:, r, i, :], xbuf[:, i, :]),
                        ld_x[0][i] if b == 0 else ld_x[b], free)
                ag.append(dve(lambda e, i=i: e.bn_aggr(mv[:, r, i, :], bn[:, r, i, :]), o, c=.07))
            st["inv"] = inv_std(r, 0, 4, ag, False)

        def n():
            r = st["r"]
            nbuf, free = ntr.take()
            nrm = [dve(lambda e, i=i: e.tensor_scalar(ntok[nbuf][:, i, :], xbuf[:, i, :], mv[:, r, i, 0:1], rs[:, r, i:i + 1],
                                                      ALU.subtract, ALU.mult), st["inv"], free) for i in range(4)]
            stat.give(r, nrm)
            st_x["used"] = nrm
            a_rdy[s] = None
            st["a"] = []
            back([K + v for v in XHAT_BACK], nbuf, nrm, consume)

        def consume(t, m, bk, op):
            def h():
                hi = act(lambda e: e.activation(AH[s][:, m, :], PS[6 + bk][:], ACT.Copy), op, a_used[s])
                lo = dve(lambda e: e.tensor_tensor(AL[s][:, m, :], PS[6 + bk][:], AH[s][:, m, :].bitcast(F32),
                                                   ALU.subtract), hi)
                st["a"] += [hi, lo]
                if m == KC - 1:
                    a_rdy[s] = st["a"]
                t2r.give(bk, hi, lo)
            at(t, h)

        if b > 0:
            before = max(base[j] for j in base if j[2] == 0 and base[j] < K)
            at(max(K - 28, before + XHAT_AT[1] + .1), load)
        at(K + XHAT_AT[0], a)
        at(K + XHAT_AT[1], n)

    st_x = {"used": "held"}

    def tail(b, d, l, K, k1, k2):
        s = 2 * (b % 2) + d
        st = {"nrm": []}
        evs, t1s = [], []

        def t1(pr):
            if pr == 0:
                st["r"], st["free"] = stat.take()
            r = st["r"]
            got = []
            for i in (2 * pr, 2 * pr + 1):
                bk, free = t1r.take()

                def f(e, i=i, bk=bk):
                    for m in range(KC):
                        o = e.transpose(PS[2 + bk][:, m * 128:(m + 1) * 128], H[s][:, m, i * 128:(i + 1) * 128], ident[:])
                    return o

                assert len(state[(b, d, l)]) == KC
                t = pe(f, state[(b, d, l)], free, c_id, c=.43)
                got.append((i, bk, t))
                t1s.append(t)
            if pr == 1:
                h_used[s] = t1s if l < 3 else "held"
            at(K + k1[pr] + .5, lambda: stats(pr, got))

        def stats(pr, got):
            r = st["r"]
            ag = []
            for i, bk, t in got:
                o = dve(lambda e, i=i, bk=bk: e.bn_stats(bn[:, r, i, :], PS[2 + bk][:]), t, st["free"])
                ag.append(dve(lambda e, i=i: e.bn_aggr(mv[:, r, i, :], bn[:, r, i, :]), o, c=.07))
            inv = inv_std(r, 2 * pr, 2 * pr + 2, ag, True)
            at(K + k1[pr] + NORM, lambda: norm(pr, got, ag, inv))

        def norm(pr, got, ag, inv):
            r = st["r"]
            if pr == 0:
                st["nt"], st["ntfree"] = ntr.take()
            for i, bk, t in got:
                o = act(lambda e, i=i, bk=bk: e.activation(ntok[st["nt"]][:, i, :], PS[2 + bk][:], ACT.Identity,
                                                           bias=nb[:, r, i:i + 1], scale=rs[:, r, i:i + 1]),
                        inv, t, ag, st["ntfree"], c=.66)
                st["nrm"].append(o)
                t1r.give(bk, o)
            if pr == 1:
                stat.give(r, *st["nrm"])
                if l < 3:
                    a_rdy[s], st["a"] = None, []
                back([K + k for k in k2], st["nt"], st["nrm"], consume)

        def consume(t, m, bk, op):
            def h():
                ev = act(lambda e: e.activation(H[s][:, m, :], PS[6 + bk][:], ACT.Identity, bias=bet[:, m:m + 1],
                                                scale=gam[:, m:m + 1]), op, ld_g, ld_b)
                evs.append(ev)
                t2r.give(bk, ev)
                if l < 3:
                    if m % 2:
                        at(t + HALVES, lambda: halves(m))
                elif m == KC - 1:
                    at(t + .7, store)
            at(t, h)

        def halves(m):
            sl = slice(m - 1, m + 1)
            hi = dve(lambda e: e.tensor_copy(AH[s][:, sl, :], H[s][:, sl, :]), evs[m - 1], evs[m], a_used[s])
            lo = dve(lambda e: e.tensor_tensor(AL[s][:, sl, :], H[s][:, sl, :], AH[s][:, sl, :].bitcast(F32),
                                               ALU.subtract), hi, c=1.14)
            st["a"] += [hi, lo]
            if m == KC - 1:
                a_rdy[s], h_rdy[s] = st["a"], evs

        def store():
            st_ = dma(f"d_xs{s}", lambda e: e.dma_start(hs[b, :, KC * d:KC * d + KC, :], H[s][:]), evs, c=5)
            h_used[s] = st_
            hs_done[(b, d)] = st_

        at(K + k1[0], lambda: t1(0))
        at(K + k1[1], lambda: t1(1))

    state = {}

    def job(b, d, l):
        s = 2 * (b % 2) + d
        K = base[(b, d, l)]
        mms = []
        if l == 0:
            state[(b, 0, 0)], state[(b, 1, 0)] = [], []
        else:
            state[(b, d, l)] = []

        def mm(m):
            bk, free = gate.take()

            def f(e):
                steps = [(w, a, k) for k in range(KC) for w, a in ((WH[l], AH[s]), (WH[l], AL[s]), (WL[l], AH[s]))]
                for j, (w, a, k) in enumerate(steps):
                    r = e.matmul(PS[bk][:], w[:, k, m * 128:(m + 1) * 128], a[:, k, :], start=(j == 0),
                                 stop=(j == len(steps) - 1))
                return r

            assert a_rdy[s] and len(w_rdy[l]) == 2 * KC, "operands are not planned yet"
            o = pe(f, a_rdy[s], w_rdy[l], free, c=2.57)
            mms.append(o)
            a_used[s] = "held"
            if m == KC - 1:
                a_used[s] = mm_done[(b, d, l)] = mms
            at(K + CHUNK * m + GATES, lambda: gates(m, bk, o))

        def gates(m, bk, o):
            c, free = chr_.take()
            t = K + CHUNK * m + GATES
            sg = act(lambda e: e.activation(zb[c][:], PS[bk][:], ACT.Sigmoid, bias=condt[:, l, m:m + 1]), o, free, ld_c)
            tn = act(lambda e: e.activation(hb[c][:], PS[bk][:], ACT.Tanh, bias=condt[:, l, m:m + 1]), o, free, ld_c)
            gate.give(bk, sg, tn)
            at(t + KEEP, lambda: keep(m, c, sg, tn))

        def keep(m, c, sg, tn):
            t = K + CHUNK * m + GATES
            aa = dve(lambda e: e.scalar_tensor_tensor(ab[c][:], zb[c][:], 1.0, tiny[:, 0:1].broadcast_to([128, S]),
                                                      ALU.subtract, ALU.max, reverse0=True), sg, c_tiny)
            vv = pool(lambda e: e.tensor_tensor(hb[c][:], zb[c][:], hb[c][:], ALU.mult), sg, tn)
            at(t + SCAN, lambda: scan(m, c, aa, vv))

        def scan(m, c, aa, vv):
            t = K + CHUNK * m + GATES
            if l == 0:
                both = []
                for dd in range(2):
                    tgt = 2 * (b % 2) + dd
                    rv = slice(None, None, -1) if dd else slice(None)
                    sc = dve(lambda e, tgt=tgt, rv=rv: e.tensor_tensor_scan(H[tgt][:, m, :][:, rv], ab[c][:, rv], hb[c][:, rv],
                                                                            0.0, ALU.mult, ALU.add), aa, vv, h_used[tgt])
                    state[(b, dd, 0)].append(sc)
                    both.append(sc)
                chr_.give(c, both)
                return
            rv = slice(None, None, -1) if d else slice(None)
            sc = dve(lambda e: e.tensor_tensor_scan(zb[c][:, rv], ab[c][:, rv], hb[c][:, rv], 0.0, ALU.mult, ALU.add), aa, vv)
            at(t + RESID, lambda: resid(m, c, sc))

        def resid(m, c, sc):
            r = pool(lambda e: e.tensor_tensor(H[s][:, m, :], H[s][:, m, :], zb[c][:], ALU.add), sc, h_rdy[s], a_rdy[s])
            state[(b, d, l)].append(r)
            chr_.give(c, r)

        for m in range(KC):
            at(K + CHUNK * m, lambda m=m: mm(m))
        if l == 0:
            tail(b, 0, 0, K, TOK_F0, BACK_F0)
            tail(b, 1, 0, K, TOK_B0, BACK_B0)
        else:
            tail(b, d, l, K, TOK, BACK)

    for j in jobs:
        if j[2] == 0:
            xhat(j[0], base[j])
        job(*j)

    AB0 = 80
    pieces = [(0, k, c) for k in range(4) for c in range(4)] + [(1, k, 0) for k in range(16)]

    def src(w, k, c):
        return fct_v[:, k, c, :] if w == 0 else pjt_v[:, k, :]

    sums = []
    stg_free = [None]

    def abs_load(n):
        w, k, c = pieces[n]
        ld = dma("d_st4", lambda e: e.dma_start(stg[:], src(w, k, c)), stg_free[0] or mm_done[(0, 0, 0)])
        at(AB0 + 6 + n * 10.0, lambda: abs_sum(n, ld))

    def abs_sum(n, ld):
        a = act(lambda e: e.activation(stg[:], stg[:], ACT.Abs, accum_out=asum[:, n:n + 1]), ld)
        sums.append(a)
        stg_free[0] = [a]

    for n in range(32):
        at(AB0 + n * 10.0, lambda n=n: abs_load(n))

    thr = []

    def totals():
        r = [dve(lambda e, w=w: e.reduce_sum(ssum[:, w:w + 1], asum[:, 16 * w:16 * w + 16], axis=AX_X), sums) for w in range(2)]
        t = pool(lambda e: e.partition_all_reduce(tot[:], ssum[:], 128, RADD), r)
        o = dve(lambda e: e.tensor_scalar(th[:], tot[:], 1.0 / (512 * HID), 1e-6, ALU.mult, ALU.add), t)
        o1 = dve(lambda e: e.tensor_scalar(nth[:], th[:], -0.5, None, ALU.mult), o)
        o2 = dve(lambda e: e.tensor_scalar(th[:], th[:], 0.5, None, ALU.mult), o1)
        thr.extend([o1, o2])

    at(AB0 + 330, totals)

    srcb = Ring(5)
    sbuf5 = [xbuf[:, i, :] for i in range(4)] + [stg[:]]
    fu_rdy, fc_rdy, pj_rdy = [], [], []

    def prep(t, ap, free_ops, work):
        def ld():
            i, free = srcb.take()
            w = [free if free is not None else [st_x["used"], sums]]
            o = dma(f"d_st{i}", lambda e: e.dma_start(sbuf5[i], ap), *w)
            at(t, lambda: go(i, o))

        def go(i, o):
            last = work(sbuf5[i], o, free_ops())
            srcb.give(i, last)

        at(t - 5, ld)

    def fuse_w(k):
        def work(buf, ld, free):
            hi = dve(lambda e: e.tensor_copy(FUH[:, k, :], buf), ld, free)
            lo = dve(lambda e: e.tensor_tensor(FUL[:, k, :], buf, FUH[:, k, :].bitcast(F32), ALU.subtract), hi)
            fu_rdy.extend([hi, lo])
            return lo
        return work

    def ternary(w, dst, rdy, eng=None, c=.4):
        def work(buf, ld, free):
            a = (eng or dve)(lambda e: e.tensor_scalar(dst, buf, th[:, w:w + 1], None, ALU.is_gt), ld, free, thr, c=c)
            o = dve(lambda e: e.scalar_tensor_tensor(dst, buf, nth[:, w:w + 1], dst.bitcast(F32), ALU.is_lt, ALU.subtract,
                                                     reverse1=True), a)
            rdy.append(o)
            return o
        return work

    last = lambda l: max(base[(b, d, l)] for b in (NB - 2, NB - 1) for d in range(2)) + 11
    of_layer = lambda l: [mm_done[(b, d, l)] for b in (NB - 2, NB - 1) for d in range(2)]
    for k in range(8):
        prep(last(1) + PREP[0] + PREP[1] * k, fwt_v[:, k, :], lambda: of_layer(1), fuse_w(k))
    for k in range(2):
        for c in range(4):
            prep(last(2) + PREP[2] + PREP[3] * (4 * k + c), fct_v[:, k, c, :], lambda: of_layer(2),
                 ternary(0, FCA[:, k, c * 512:(c + 1) * 512], fc_rdy))
    for k in range(16):
        prep(END + PREP[4] + PREP[5] * k, pjt_v[:, k, :],
             (lambda: of_layer(3)) if k < 8 else (lambda: mm_done[(NB - 1, 0, 3)]), ternary(1, PJ[k], pj_rdy, pool, 1.54))
    for k in range(2):
        for c in range(4):
            prep(base[(NB - 1, 1, 3)] + 11 + PREP[6] + PREP[7] * (4 * k + c), fct_v[:, 2 + k, c, :], lambda: mm_done[(NB - 1, 1, 3)],
                 ternary(0, FCB[:, k, c * 512:(c + 1) * 512], fc_rdy))

    NU = NB * 4
    V0 = END + START2
    over = lambda ring, *idx: [lambda i=i: ring.free[i] for i in idx]
    e6_ops = lambda: [mm_done[(NB - 2, d, 3)] for d in range(2)]
    E6 = max(base[(NB - 2, d, 3)] for d in range(2)) + 11.2
    hcr = Ring(2, [lambda: e6_ops()] * 2)
    xrr = Ring(2, [lambda: e6_ops()] * 2)
    hlr = Ring(2, [lambda: e6_ops()] * 2)
    x1r = Ring(3, over(chr_, 2, 0, 1))
    n1r = Ring(2, over(chr_, 2, 0))
    xhr = Ring(2, [lambda: h_used[0]] * 2)
    ur = Ring(4, [lambda: [h_used[2], h_used[3]]] * 4)
    gr = Ring(2, over(ntr, 0, 1))
    obr = Ring(2, over(chr_, 0, 1))
    fubank = Ring(1, over(gate, 0))
    t1bank = Ring(1, over(gate, 1))
    pjbank = Ring(1, over(t1r, 0))
    fcbank = Ring(2, over(t1r, 1, 2))
    t2bank = Ring(3, over(t1r, 3) + over(t2r, 0, 1))
    rows = {}
    outs = []

    def load_rows():
        rows["fbb"] = dma("d_fb", lambda e: e.dma_start(fbb[:], fb.partition_broadcast(128)), hs_done[(0, 0)])

    def load_w_row():
        rows["w"] = dma("d_row", lambda e: e.dma_start(wrow[:], lnw.partition_broadcast(128)), h_used[1], c=5)

    at(END - 22, load_rows)
    at(END + 24, load_w_row)

    def load_b():
        rows["b"] = dma("d_lnb", lambda e: e.dma_start(lnbt[:], lnb), hs_done[(0, 0)])

    at(END - 21, load_b)

    def bias_row():
        bk, free = pjbank.take()
        ring = Ring(2, [chr_.free[1]] * 2)
        m = None
        for k in range(16):
            i, fr = ring.take()
            hi = dve(lambda e, k=k, i=i: e.tensor_copy(bh[i][:, 0, :], lnbt[:, k:k + 1].broadcast_to([128, 128])), rows["b"],
                     fr, c=.2)
            lo = dve(lambda e, k=k, i=i: e.tensor_tensor(bh[i][:, 1, :], lnbt[:, k:k + 1].broadcast_to([128, 128]),
                                                         bh[i][:, 0, :].bitcast(F32), ALU.subtract), hi, c=.2)

            def f(e, k=k, i=i):
                e.matmul(PS[2][:], bh[i][:, 0, :], PJ[k], start=(k == 0), stop=False)
                return e.matmul(PS[2][:], bh[i][:, 1, :], PJ[k], start=False, stop=(k == 15))

            assert len(pj_rdy) == 16
            m = pe(f, hi, lo, pj_rdy, free, after=m, c=.43)
            ring.give(i, m)
        o = act(lambda e: e.activation(cB[:], PS[2][:], ACT.Copy), m, chr_.free[2])
        rows["cB"] = o
        pjbank.give(bk, o)

    at(END + CB_AT, bias_row)

    def unit(u):
        V = V0 + U * u
        b = u // 4
        st = {}
        fcs, t2s = [], []

        def load():
            i, free = hcr.take()
            st["hc"] = i
            st["ld"] = dma(f"d_hc{i}", lambda e: e.dma_start(hc[i][:], hs[b, :, :, (u % 4) * 128:(u % 4 + 1) * 128]), free,
                           hs_done[(b, 0)], hs_done[(b, 1)])
            i2, free = xrr.take()
            st["xr"] = i2
            st["ldx"] = dma(f"d_x{i2}", lambda e: e.dma_start(xr[i2][:], x[b, (u % 4) * 128:(u % 4 + 1) * 128, :]), free)

        def split():
            i, free = hlr.take()
            st["hl"] = i
            hi = dve(lambda e: e.tensor_copy(hch[i][:], hc[st["hc"]][:]), st["ld"], free)
            lo = dve(lambda e: e.tensor_tensor(hcl[i][:], hc[st["hc"]][:], hch[i][:].bitcast(F32), ALU.subtract), hi, c=1.14)
            hcr.give(st["hc"], lo)
            st["split"] = [hi, lo]

        def addx():
            j = st["xr"]
            st["xf"] = pool(lambda e: e.tensor_tensor(xf[j][:], xr[j][:], fbb[:], ALU.add), st["ldx"], rows["fbb"], free_xf[j])

        def fuse():
            bk, free = fubank.take()
            i = st["hl"]

            def f(e):
                n = 0
                for k in range(8):
                    for a, w in ((hch, FUH), (hch, FUL), (hcl, FUH)):
                        r = e.matmul(PS[0][:], a[i][:, k, :], w[:, k, :], start=(n == 0), stop=(n == 23))
                        n += 1
                return r

            assert len(fu_rdy) == 16
            o = pe(f, st["split"], fu_rdy, free, c=5.13)
            hlr.give(i, o)
            st["fuse"] = o

        def resid():
            i, free = x1r.take()
            st["x1"] = i
            j = st["xr"]
            o = dve(lambda e: e.tensor_tensor(x1[i][:], PS[0][:], xf[j][:], ALU.add), st["fuse"], st["xf"], free)
            fubank.give(0, o)
            free_xf[j] = o
            xrr.give(j, st["xf"])
            r, free = stat.take()
            st["r1"] = r
            o = dve(lambda e: e.bn_stats(bn[:, r, 0, :], x1[i][:]), o, free)
            o = dve(lambda e: e.bn_aggr(mv[:, r, 0, :], bn[:, r, 0, :]), o)
            st["inv1"] = inv_std(r, 0, 1, [o], False)

        def norm():
            i, r = st["x1"], st["r1"]
            j, free = n1r.take()
            st["n1"] = j
            st["nrm"] = dve(lambda e: e.tensor_scalar(n1[j][:], x1[i][:], mv[:, r, 0, 0:1], rs[:, r, 0:1], ALU.subtract,
                                                      ALU.mult), st["inv1"], free, c=.33)
            stat.give(r, st["nrm"])

        def t1():
            bk, free = t1bank.take()
            j = st["n1"]

            def f(e):
                for m in range(4):
                    o = e.transpose(PS[1][:, m * 128:(m + 1) * 128], n1[j][:, m * 128:(m + 1) * 128], ident[:])
                return o

            o = pe(f, st["nrm"], free, c=.43)
            n1r.give(j, o)
            st["t1"] = o

        def t1out():
            i, free = xhr.take()
            st["xh"] = i
            hi = act(lambda e: e.activation(xh[i][:].rearrange("p a t -> p (a t)"), PS[1][:], ACT.Copy), st["t1"], free, c=.48)
            lo = dve(lambda e: e.tensor_tensor(xl[i][:].rearrange("p a t -> p (a t)"), PS[1][:],
                                               xh[i][:].rearrange("p a t -> p (a t)").bitcast(F32), ALU.subtract), hi)
            t1bank.give(0, hi, lo)
            st["xhl"] = [hi, lo]

        def addc():
            i = st["x1"]
            st["xc"] = pool(lambda e: e.tensor_tensor(x1[i][:], x1[i][:], cB[:], ALU.add), st["nrm"], rows["cB"])

        def fc(n):
            bk, free = fcbank.take()
            i = st["xh"]

            def f(e):
                c = 0
                for k in range(4):
                    wk = FCA[:, k, n * 512:(n + 1) * 512] if k < 2 else FCB[:, k - 2, n * 512:(n + 1) * 512]
                    for a in (xh, xl):
                        r = e.matmul(PS[3 + bk][:], a[i][:, k, :], wk, start=(c == 0), stop=(c == 7))
                        c += 1
                return r

            assert len(fc_rdy) == 16
            o = pe(f, st["xhl"], fc_rdy, free, c=1.71)
            fcs.append(o)
            if n == 3:
                xhr.give(i, fcs)
            at(V + 5.1 + 1.7 * n + 1.75, lambda: gelu(n, bk, o))

        def gelu(n, bk, o):
            if n == 0:
                st["g"], st["gfree"] = gr.take()
                st["r2"], st["sfree"] = stat.take()
                st["bn"] = []
            i, r = st["g"], st["r2"]
            a = act(lambda e: e.activation(g[i][:, n * 512:(n + 1) * 512], PS[3 + bk][:], ACT.Gelu), o, st["gfree"], c=.48)
            fcbank.give(bk, a)
            st["bn"].append(dve(lambda e: e.bn_stats(bn[:, r, n, :], g[i][:, n * 512:(n + 1) * 512]), a, st["sfree"]))
            if n == 3:
                o = dve(lambda e: e.bn_aggr(mv[:, r, 0, :], bn[:, r, :, :]), st["bn"])
                st["ag2"] = o
                st["inv2"] = inv_std(r, 0, 1, [o], False)

        def scale(n):
            i, r = st["g"], st["r2"]
            sl = slice(n * 512, (n + 1) * 512)
            o = dve(lambda e: e.scalar_tensor_tensor(g[i][:, sl], g[i][:, sl], mv[:, r, 0, 0:1], wrow[:, sl],
                                                     ALU.subtract, ALU.mult), st["ag2"], st["bn"], rows["w"])
            st.setdefault("sc", []).append(o)

        def t2(n):
            bk, free = t2bank.take()
            i = st["g"]

            def f(e):
                for m in range(4):
                    c = n * 512 + m * 128
                    o = e.transpose(PS[5 + bk][:, m * 128:(m + 1) * 128], g[i][:, c:c + 128], ident[:])
                return o

            o = pe(f, st["sc"][n], free, c=.43)
            t2s.append(o)
            if n == 3:
                gr.give(i, t2s)
            at(t2k[n] + V + .3, lambda: t2out(n, bk, o))

        def t2out(n, bk, o):
            j, free = ur.take()
            hi = act(lambda e: e.activation(uth[j][:].rearrange("p a t -> p (a t)"), PS[5 + bk][:], ACT.Copy), o, free, c=.48)
            lo = dve(lambda e: e.tensor_tensor(utl[j][:].rearrange("p a t -> p (a t)"), PS[5 + bk][:],
                                               uth[j][:].rearrange("p a t -> p (a t)").bitcast(F32), ALU.subtract), hi)
            t2bank.give(bk, hi, lo)
            st[("ut", n)] = (j, [hi, lo])

        def proj(n):
            if n == 0:
                bk, st["pfree"] = pjbank.take()
            j, rdy = st[("ut", n)]

            def f(e):
                for m in range(4):
                    for a in (uth, utl):
                        r = e.matmul(PS[2][:], a[j][:, m, :], PJ[4 * n + m], start=(n == 0 and m == 0 and a is uth),
                                     stop=(n == 3 and m == 3 and a is utl))
                return r

            assert len(pj_rdy) == 16
            o = pe(f, rdy, pj_rdy, st["pfree"], after=st.get("pj"), c=1.71)
            ur.give(j, o)
            st["pj"] = o

        def final():
            i, free = obr.take()
            r, k = st["r2"], st["x1"]
            o = dve(lambda e: e.scalar_tensor_tensor(ob[i][:], PS[2][:], rs[:, r, 0:1], x1[k][:], ALU.mult, ALU.add),
                    st["pj"], st["inv2"], st["xc"], free)
            pjbank.give(0, o)
            stat.give(r, o)
            x1r.give(k, o)
            d = dma(f"d_o{i}", lambda e: e.dma_start(out[b, (u % 4) * 128:(u % 4 + 1) * 128, :], ob[i][:]), o)
            obr.give(i, d)
            outs.append(d)

        t2k = [25.0, 25.05, 32.0, 33.7]
        pjk = [32.1, 33.8, 35.5, 37.2]
        at(max(V - 32, E6 + .01 * u), load)
        at(max(V - 26, E6 + 2), split)
        at(V - 20, fuse)
        at(V - 17, addx)
        at(V - 14.8, resid)
        at(V - 11, norm)
        at(V - 8, t1)
        at(V - 7.6, t1out)
        at(max(V - 2, END + CB_AT + .5 + .1 * u), addc)
        for n in range(4):
            at(V + 5.1 + 1.7 * n, lambda n=n: fc(n))
            at(V + 14.5 + .6 * n, lambda n=n: scale(n))
            at(V + t2k[n], lambda n=n: t2(n))
            at(V + pjk[n], lambda n=n: proj(n))
        at(V + 39.2, final)

    free_xf = [None, None]
    for u in range(NU):
        unit(u)

    while plan:
        plan.sort(key=lambda p: p[:2])
        t, _, step = plan.pop()
        now[0] = -t
        step()
    q.arrange()

    totals_ = q.count()
    sems = {n: ctx.enter_context(nc.semaphore("s_" + n)) for n in totals_}
    block = ctx.enter_context(nc.Block())

    @block.tensor
    def _(e):
        q.emit("pe", e, sems)

    @block.scalar
    def _(e):
        q.emit("act", e, sems)

    @block.vector
    def _(e):
        q.emit("dve", e, sems)

    @block.gpsimd
    def _(e):
        q.emit("pool", e, sems)

    @block.sync
    def _(e):
        q.emit("sp", e, sems)
        for name, value in totals_.items():
            if name.startswith("d_"):
                e.wait_ge(sems[name], value)

    ctx.close()


def kernel(**inputs):
    import numpy as _np
    import concourse.bacc as _bacc
    from concourse import mybir as _mybir
    from concourse.bass_utils import run_bass_kernel_spmd as _run

    a = {k: _np.asarray(v) for k, v in inputs.items()}
    cols = lambda v: v.reshape(-1, 128).T
    data = {
        "x": a["x"],
        "wt": a["ctx_1024"][:L].transpose(0, 2, 1),
        "cond": a["cond_1024"][:L].reshape(L, KC, 128).transpose(2, 0, 1),
        "fwt": a["L0_xcond_fusion_W"].T,
        "fb": a["L0_xcond_fusion_b"],
        "gamma": cols(a["L0_xcond_ln_gamma"]),
        "beta": cols(a["L0_xcond_ln_beta"]),
        "fct": a["L0_ffn_W_fc"].T,
        "lnw": a["L0_ffn_ln_w"],
        "lnb": cols(a["L0_ffn_ln_b"]),
        "pjt": a["L0_ffn_W_proj"].T,
    }
    nc = _bacc.Bacc("TRN2", target_bir_lowering=False, num_devices=1)
    arrays, args = {}, []
    for name, v in data.items():
        v = _np.ascontiguousarray(v)
        arrays[f"in_{name}"] = v
        args.append(nc.dram_tensor(f"in_{name}", v.shape, _mybir.dt.from_np(v.dtype), kind="ExternalInput").ap())
    o = nc.dram_tensor("out_0", (NB, S, 512), _mybir.dt.float32, kind="ExternalOutput").ap()
    pixart_block(nc, *args, o)
    r = _run(nc, [arrays], core_ids=[0])
    return r.results[0]["out_0"]
```
